# Optimizing a Trainium2 kernel written in Bass

```python
import numpy as np
import jax
import jax.numpy as jnp

def _softmax(x, axis=-1):
    return jax.nn.softmax(x, axis=axis)

def _gelu(x):
    return jax.nn.gelu(x, approximate=True)

def _silu(x):
    return jax.nn.silu(x)

def _sigmoid(x):
    return jax.nn.sigmoid(x)

def _layernorm(x, axis=-1, eps=1e-05):
    m = jnp.mean(x, axis=axis, keepdims=True)
    v = jnp.var(x, axis=axis, keepdims=True)
    return (x - m) / jnp.sqrt(v + eps)

def _scatter_add(tgt, idx, src, axis=0):
    return tgt.at[idx].add(src)

def _segment_sum(src, seg, n):
    return jax.ops.segment_sum(src, seg, n)
kernel_name = 'mk_xattn_ffn_d1_seqx_r8_f4747b'

def setup_inputs(seed: int=0):
    np.random.seed(seed)
    _w = jnp.asarray

    def _rec_inputs():
        import jax
        import jax.numpy as jnp
        _rk = jax.random.key(seed)
        x = 7.22e-05 + 1 * jax.random.normal(jax.random.fold_in(_rk, 1), (8, 256, 128), jnp.float32)
        _lenS = 256 - jax.random.randint(jax.random.fold_in(_rk, 7), (8,), 0, max(1, 256 // 4) + 1, jnp.int32)
        _lenS2 = 256 - jax.random.randint(jax.random.fold_in(_rk, 8), (8,), 0, max(1, 256 // 4) + 1, jnp.int32)
        _ctx_1024P = jax.random.normal(jax.random.fold_in(_rk, 11), (8, 16, 128), jnp.float32)
        _ctx_1024c = jax.random.dirichlet(jax.random.fold_in(_rk, 511), 0.3 * jnp.ones((16,), jnp.float32), (8, 256))
        _ctx_1024t = jnp.einsum('bsk,bkd->bsd', _ctx_1024c, _ctx_1024P)
        _ctx_1024t = _ctx_1024t * jax.lax.rsqrt(jnp.mean(jnp.square(_ctx_1024t)) + 1e-12) * 0.953939
        ctx_1024 = 4.13588e-05 + 0.999923 * (_ctx_1024t + 0.3 * jax.random.normal(jax.random.fold_in(_rk, 611), (8, 256, 128), jnp.float32))
        _validS = jnp.arange(256)[None, :] < _lenS[:, None]
        _validS2 = jnp.arange(256)[None, :] < _lenS2[:, None]
        _causal = jnp.tril(jnp.ones((256, 256), dtype=bool))
        mask_BxS2_bf1 = jnp.ones((8, 256), dtype=bool)
        return (x, ctx_1024, mask_BxS2_bf1)
    x, ctx_1024, mask_BxS2_bf1 = _rec_inputs()

    def _L0_xattn_setup():
        import jax, jax.numpy as jnp
        import numpy as np
        B, S, D, H = (4, 256, 128, 16)
        DK = D // H
        key = jax.random.key(seed)
        ks = jax.random.split(key, 7)
        scale = 1.0 / np.sqrt(D)
        return {'query': jax.random.normal(ks[0], (B, S, D), dtype=jnp.float32), 'key': jax.random.normal(ks[1], (B, S, D), dtype=jnp.float32), 'value': jax.random.normal(ks[2], (B, S, D), dtype=jnp.float32), 'mask': jnp.ones((B, S), dtype=bool), 'w_q': jax.random.normal(ks[3], (D, D), dtype=jnp.float32) * scale, 'w_k': jax.random.normal(ks[4], (D, D), dtype=jnp.float32) * scale, 'w_v': jax.random.normal(ks[5], (D, D), dtype=jnp.float32) * scale, 'w_o': jax.random.normal(ks[6], (D, D), dtype=jnp.float32) * scale}
    _L0_xattn_all = _L0_xattn_setup()
    _L0_xattn_in = {k: v for k, v in _L0_xattn_all.items() if k in ('w_q', 'w_k', 'w_v', 'w_o')}
    del _L0_xattn_all

    def _L0_ffn_setup():
        import jax, jax.numpy as jnp
        import numpy as np
        DIM = 128
        HIDDEN = 384
        SCALE = 1.0 / 127.0

        def _dequant(w_int, dtype):
            return w_int.astype(dtype) * jnp.asarray(SCALE, dtype)
        key = jax.random.key(seed)
        k_x, k_g, k_u, k_d = jax.random.split(key, 4)
        x = jax.random.normal(k_x, (4, 256, DIM), dtype=jnp.float32)
        w_gate = jax.random.randint(k_g, (HIDDEN, DIM), -127, 128, dtype=jnp.int32)
        w_up = jax.random.randint(k_u, (HIDDEN, DIM), -127, 128, dtype=jnp.int32)
        w_down = jax.random.randint(k_d, (DIM, HIDDEN), -127, 128, dtype=jnp.int32)
        return {'x': x, 'w_gate': w_gate, 'w_up': w_up, 'w_down': w_down}
    _L0_ffn_all = _L0_ffn_setup()
    _L0_ffn_in = {k: v for k, v in _L0_ffn_all.items() if k in ('w_gate', 'w_up', 'w_down')}
    del _L0_ffn_all
    return {'x': x, 'ctx_1024': ctx_1024, 'mask_BxS2_bf1': mask_BxS2_bf1, 'L0_xattn_w_q': _L0_xattn_in['w_q'], 'L0_xattn_w_k': _L0_xattn_in['w_k'], 'L0_xattn_w_v': _L0_xattn_in['w_v'], 'L0_xattn_w_o': _L0_xattn_in['w_o'], 'L0_ffn_w_gate': _L0_ffn_in['w_gate'], 'L0_ffn_w_up': _L0_ffn_in['w_up'], 'L0_ffn_w_down': _L0_ffn_in['w_down']}

def reference(x, ctx_1024, mask_BxS2_bf1, L0_xattn_w_q, L0_xattn_w_k, L0_xattn_w_v, L0_xattn_w_o, L0_ffn_w_gate, L0_ffn_w_up, L0_ffn_w_down):
    import jax
    import jax.numpy as jnp

    def _L0_xattn_ref(query, key, value, mask, w_q, w_k, w_v, w_o):
        import jax, jax.numpy as jnp
        import numpy as np
        B, S, D, H = (4, 256, 128, 16)
        DK = D // H
        b, tgt, d = query.shape
        src = key.shape[1]
        Q = (query @ w_q.T).reshape(b, tgt, H, DK).transpose(0, 2, 1, 3)
        K = (key @ w_k.T).reshape(b, src, H, DK).transpose(0, 2, 1, 3)
        V = (value @ w_v.T).reshape(b, src, H, DK).transpose(0, 2, 1, 3)
        scores = jnp.einsum('bhtd,bhsd->bhts', Q, K) / np.sqrt(DK)
        m = mask[:, None, None, :]
        scores = jnp.where(m, scores, -jnp.inf)
        attn = jax.nn.softmax(scores, axis=-1)
        out = jnp.einsum('bhts,bhsd->bhtd', attn, V)
        out = out.transpose(0, 2, 1, 3).reshape(b, tgt, d)
        return out @ w_o.T

    def _L0_ffn_ref(x, w_gate, w_up, w_down):
        import jax, jax.numpy as jnp
        import numpy as np
        DIM = 128
        HIDDEN = 384
        SCALE = 1.0 / 127.0

        def _dequant(w_int, dtype):
            return w_int.astype(dtype) * jnp.asarray(SCALE, dtype)
        wg = _dequant(w_gate, x.dtype)
        wu = _dequant(w_up, x.dtype)
        wd = _dequant(w_down, x.dtype)
        gate = jnp.einsum('bsd,hd->bsh', x, wg)
        up = jnp.einsum('bsd,hd->bsh', x, wu)
        h = jax.nn.silu(gate) * up
        return jnp.einsum('bsh,dh->bsd', h, wd)
    x = x + _L0_xattn_ref(_layernorm(x, axis=-1), ctx_1024, ctx_1024, mask_BxS2_bf1, L0_xattn_w_q, L0_xattn_w_k, L0_xattn_w_v, L0_xattn_w_o)
    x = x + _L0_ffn_ref(_layernorm(x, axis=-1), L0_ffn_w_gate, L0_ffn_w_up, L0_ffn_w_down)
    return x

_drawn_inputs = setup_inputs


def setup_inputs(seed=0):
    import zlib

    import numpy as np

    out = dict(_drawn_inputs(seed))
    spreads = {}
    factors = {}
    for name, (base, spread) in spreads.items():
        noise = np.random.default_rng([zlib.crc32(name.encode()), seed]).standard_normal(out[name].shape)
        drawn = base * np.exp(spread * noise) if base else spread * noise
        out[name] = jnp.asarray(drawn.astype(out[name].dtype))
    for name, factor in factors.items():
        out[name] = (out[name] * factor).astype(out[name].dtype)
    return out
```

```python
from contextlib import ExitStack

import concourse.bass as bass
from concourse import mybir

F32 = mybir.dt.float32
BF16 = mybir.dt.bfloat16
I32 = mybir.dt.int32
U8 = mybir.dt.uint8
ALU = mybir.AluOpType
ACT = mybir.ActivationFunctionType
AX = mybir.AxisListType

P = 128
HEADS = 16
DK = 8
PARTS = 3
PAIRS = ((0, 0), (0, 1), (0, 2), (1, 0), (1, 1), (2, 0))
MASK_ROW = DK * len(PAIRS)
MAX_ROWS = 96
SHIFT_ROW = 96
ROWS = SHIFT_ROW + 2
STAGES = 3
RING = 8
LANES = 4
VCOLS = 32
WEIGHT_SCALE = 1.0 / 127.0
EPS = 1e-5
ONES_PAIR = 1.0 + 0x3F80 / 2.0**23


class Step:

    def __init__(self, base, u, registers=None):
        self.base, self.u, self.registers = base, u, registers

    def count(self, c, unit=1):
        n = self.u + c + 1
        return (self.base + n) * unit if self.registers is None else self.registers[n, unit]

    def stage(self, c):
        return ((self.base if self.registers is None else 1) + self.u + c) % STAGES


def build(nc, x, ctxT, mask, wqT, wkT, wvT, woT, wguT, wdT, out):
    B, S, D = x.shape
    TT = S // P
    HALF = HEADS // 2
    CH = wdT.shape[1]
    SCALE = float(DK) ** -0.5

    with ExitStack() as ctx:
        def sb(name, shape, dt):
            return ctx.enter_context(nc.sbuf_tensor(name, shape, dt))

        def bank(name):
            return ctx.enter_context(nc.psum_tensor(name, [P, 512], F32))

        def sem(name):
            return ctx.enter_context(nc.semaphore(name))

        score_bank = [bank(f"score_bank{i}") for i in range(2)]
        max_bank = [bank(f"max_bank{i}") for i in range(2)]
        pv_bank = [bank(f"pv_bank{i}") for i in range(2)]
        bank_a, bank_b = bank("bank_a"), bank("bank_b")

        ident = sb("ident", [P, P], F32)
        ident_bf = sb("ident_bf", [P, P], BF16)
        wq = sb("wq", [P, D], F32)
        wk = sb("wk", [P, D], F32)
        wv = sb("wv", [P, D], F32)
        wo = sb("wo", [P, D], F32)
        wgu_int = sb("wgu_int", [P, CH, 2, P], I32)
        wd_int = sb("wd_int", [P, CH, D], I32)
        wgu = sb("wgu", [P, CH, 2, P], F32)
        wd = sb("wd", [P, CH, D], F32)
        minus_half = sb("minus_half", [P, TT], F32)
        mask_u8 = sb("mask_u8", [B, S], U8)
        mask_f = sb("mask_f", [B, S], F32)
        mask_bias = sb("mask_bias", [B, S], BF16)
        mask_row = sb("mask_row", [1, B * S], BF16)
        x_in = sb("x_in", [P, STAGES, TT, D], F32)
        x_res = sb("x_res", [P, STAGES, TT, D], F32)
        ctx_t = sb("ctx_t", [P, STAGES, S], F32)
        q_ops = [sb(f"q_ops{i}", [P, HEADS, S], BF16) for i in range(STAGES)]
        k_ops = [sb(f"k_ops{i}", [P, HEADS, S], BF16) for i in range(STAGES)]
        v_ops = [sb(f"v_ops{i}", [P, TT, HEADS, VCOLS], F32) for i in range(STAGES)]
        k_parts = sb("k_parts", [P, PARTS, S], BF16)
        q_parts = sb("q_parts", [P, PARTS, S], BF16)
        k_rest = sb("k_rest", [P, S], F32)
        q_rest = sb("q_rest", [P, S], F32)
        stats = sb("stats", [P, 2, TT, 6], F32)
        moments = sb("moments", [P, 2, TT, 2], F32)
        var_eps = sb("var_eps", [P, 2, TT], F32)
        rstd = sb("rstd", [P, 2, TT], F32)
        shift = sb("shift", [P, 2, TT], F32)
        xn = sb("xn", [P, 2, TT, D], F32)
        xn_t = sb("xn_t", [P, 2, S], F32)
        neg_max = sb("neg_max", [P, 2, TT, HALF], F32)
        max_parts = sb("max_parts", [P, 2, TT, 2, HALF], BF16)
        max_t = [sb(f"max_t{g}", [2 * HALF, S], BF16) for g in range(2)]
        probs = sb("probs", [P, RING, TT, S], F32)
        pv_t = sb("pv_t", [P, 2, S], F32)
        recip = sb("recip", [P, 2 * TT, LANES, 2], F32)
        attn = sb("attn", [P, 2 * TT, 2, LANES, DK], F32)
        attn_t = sb("attn_t", [P, S], F32)
        x1 = sb("x1", [P, TT, D], F32)
        tanh = sb("tanh", [P, 2, S], F32)
        gated = sb("gated", [P, 2, S], F32)
        hidden = sb("hidden", [P, CH, S], F32)
        y = sb("y", [P, TT, D], F32)

        wk_in, wq_in, wv_in, wo_in, wgu_in, wd_in = (sem(f"{w}_in") for w in ("wk", "wq", "wv", "wo", "wgu", "wd"))
        mask_in, mask_row_in = sem("mask_in"), sem("mask_row_in")
        x_loaded, ctx_loaded, res_loaded = sem("x_loaded"), sem("ctx_loaded"), sem("res_loaded")
        k_spread, q_spread = sem("k_spread"), sem("q_spread")
        shift_spread = [sem(f"shift_spread{g}") for g in range(2)]
        stored = sem("stored")
        K_SPREAD, Q_SPREAD = 16 * (len(PAIRS) + 1), 16 * len(PAIRS)
        ident_zero, ident_ready = sem("ident_zero"), sem("ident_ready")
        ops_filled = [sem(f"ops_filled{i}") for i in range(STAGES)]
        v_zero, v_filled, consts_ready = sem("v_zero"), sem("v_filled"), sem("consts_ready")
        mask_sub, mask_ready = sem("mask_sub"), sem("mask_ready")
        weights_ready = sem("weights_ready")
        scores_ready = [sem(f"scores_ready{k}") for k in range(HEADS)]
        max_scores_ready = [sem(f"max_scores_ready{k}") for k in range(HEADS)]
        pv_done = [sem(f"pv_done{q}") for q in range(HEADS // LANES)]
        k_proj, v_proj, q_proj = sem("k_proj"), sem("v_proj"), sem("q_proj")
        xn_turned = [sem("xn1_turned"), sem("xn2_turned")]
        pv_turned, attn_turned, attn_proj = sem("pv_turned"), sem("attn_turned"), sem("attn_proj")
        max_turned = [sem(f"max_turned{g}") for g in range(2)]
        gate_up = [sem(f"gate_up{c}") for c in range(CH)]
        down_proj = sem("down_proj")
        probs_ready = [sem(f"probs_ready{k}") for k in range(HEADS)]
        k_part1, k_part2, q_part1, q_part2 = sem("k_part1"), sem("k_part2"), sem("q_part1"), sem("q_part2")
        v_ready = sem("v_ready")
        xn_t_ready = [sem("xn1_t_ready"), sem("xn2_t_ready")]
        pv_copied = [sem(f"pv_copied{g}") for g in range(2)]
        attn_t_ready = sem("attn_t_ready")
        max_t_ready = [sem(f"max_t_ready{g}") for g in range(2)]
        tanh_ready = [sem(f"tanh_ready{c}") for c in range(CH)]
        max_done = [sem(f"max_done{k}") for k in range(HEADS)]
        stats_done = [sem("stats1_done"), sem("stats2_done")]
        moments_done = [sem("moments1_done"), sem("moments2_done")]
        k_rest_done, q_rest_done = sem("k_rest_done"), sem("q_rest_done")
        max_part1 = [sem(f"max_part1_{g}") for g in range(2)]
        max_part2 = [sem(f"max_part2_{g}") for g in range(2)]
        recip_done, attn_done, x1_done = sem("recip_done"), sem("attn_done"), sem("x1_done")
        gated_done = [sem(f"gated_done{c}") for c in range(CH)]
        hidden_done = [sem(f"hidden_done{c}") for c in range(CH)]
        y_done = sem("y_done")
        var_done = [sem("var1_done"), sem("var2_done")]
        rstd_done = [sem("rstd1_done"), sem("rstd2_done")]
        shift_done = [sem("shift1_done"), sem("shift2_done")]
        xn_done = [sem("xn1_done"), sem("xn2_done")]
        k_part3, q_part3 = sem("k_part3"), sem("q_part3")

        block = ctx.enter_context(nc.Block())

        def wait(eng, s, n):
            if not isinstance(n, int) or n > 0:
                eng.wait_ge(s, n)

        def settle(eng):
            eng.wait_ge(consts_ready, 1)

        def steps(eng, step, *units):
            step(Step(0, 0), False, True, True, True)
            with eng.Fori(0, (B - 2) // STAGES) as i:
                registers = {(n, unit): eng.snap((i * STAGES + 1 + n) * unit)
                             for unit in units for n in range(STAGES + 3)}
                for value in registers.values():
                    eng.to_reg(value)
                for u in range(STAGES):
                    step(Step(i * STAGES + 1, u, registers), True, True, True, True)
            step(Step(B - 1, 0), True, True, False, False)
            step(Step(B, 0), True, False, False, False)


        @block.sync
        def _(sp):
            def load(at, c):
                b = at.base + at.u + c
                b = b if isinstance(b, int) else b & (B - 1)
                settle(sp)
                wait(sp, x_loaded, at.count(c - 1, 16))
                wait(sp, xn_done[0], at.count(c - STAGES))
                sp.dma_start(x_in[:, at.stage(c)], x[b].rearrange("(t p) d -> p t d", p=P)).then_inc(x_loaded, 16)
                settle(sp)
                wait(sp, ctx_loaded, at.count(c - 1, 16))
                wait(sp, v_proj, at.count(c - STAGES))
                sp.dma_start(ctx_t[:, at.stage(c)], ctxT[b]).then_inc(ctx_loaded, 16)

            def spread_k(at, c):
                b = at.base + at.u + c
                b = b if isinstance(b, int) else b & (B - 1)
                ops = k_ops[at.stage(c)]
                settle(sp)
                wait(sp, scores_ready[HEADS - 1], at.count(c - STAGES))
                sp.dma_start(ops[MASK_ROW:MASK_ROW + 1],
                             mask_row[0:1, bass.ds(b * S, S)].rearrange("o (n s) -> o n s", n=1)
                             .broadcast_to([1, HEADS, S])).then_inc(k_spread, 16)
                wait(sp, k_part3, at.count(c))
                for n, (_, part) in enumerate(PAIRS):
                    sp.dma_start(ops[DK * n:DK * (n + 1)], k_parts[:, part]).then_inc(k_spread, 16)

            def spread_q(at, c):
                ops = q_ops[at.stage(c)]
                wait(sp, q_part3, at.count(c))
                for n, (part, _) in enumerate(PAIRS):
                    sp.dma_start(ops[DK * n:DK * (n + 1)], q_parts[:, part]).then_inc(q_spread, 16)

            def spread_shift(at, c, g):
                wait(sp, max_t_ready[g], at.count(c))
                sp.dma_start(q_ops[at.stage(c)][SHIFT_ROW:ROWS, HALF * g:HALF * (g + 1)],
                             max_t[g][:, :]).then_inc(shift_spread[g], 16)

            load(Step(0, 0), 0)
            sp.dma_start(mask_u8[:, :], mask).then_inc(mask_in, 16)
            load(Step(0, 0), 1)
            sp.wait_ge(mask_ready, 1)
            sp.dma_start(mask_row[0:1, :], mask_bias[:, :]).then_inc(mask_row_in, 16)
            load(Step(0, 0), 2)
            sp.wait_ge(mask_row_in, 16)
            sp.wait_ge(ops_filled[0], 3)
            spread_k(Step(0, 0), 0)
            spread_q(Step(0, 0), 0)
            sp.dma_start(wgu_int[:, :, :, :], wguT).then_inc(wgu_in, 16)
            sp.dma_start(wd_int[:, :, :], wdT).then_inc(wd_in, 16)
            sp.dma_start(wo[:, :], woT).then_inc(wo_in, 16)
            sp.wait_ge(ops_filled[1], 3)
            spread_k(Step(0, 0), 1)
            spread_q(Step(0, 0), 1)
            spread_shift(Step(0, 0), 0, 0)
            sp.wait_ge(ops_filled[2], 3)

            def step(at, before, now, ahead, next2):
                if now:
                    spread_shift(at, 0, 1)
                if next2:
                    load(at, 3)
                    spread_k(at, 2)
                if now:
                    b = at.base + at.u
                    settle(sp)
                    wait(sp, res_loaded, at.count(-1, 16))
                    sp.dma_start(x_res[:, at.stage(0)], x[b].rearrange("(t p) d -> p t d", p=P))\
                        .then_inc(res_loaded, 16)
                if next2:
                    spread_q(at, 2)
                if ahead:
                    spread_shift(at, 1, 0)
                if before:
                    b = at.base + at.u - 1
                    settle(sp)
                    wait(sp, y_done, at.count(-1))
                    sp.dma_start(out[b].rearrange("(t p) d -> p t d", p=P), y[:, :, :]).then_inc(stored, 16)
                    settle(sp)
                    wait(sp, stored, at.count(-1, 16))

            steps(sp, step, 1, 16)
            sp.wait_ge(k_spread, (B + 1) * K_SPREAD)
            sp.wait_ge(q_spread, (B + 1) * Q_SPREAD)
            sp.wait_ge(x_loaded, (B + 2) * 16)
            sp.wait_ge(ctx_loaded, (B + 2) * 16)

        @block.tensor
        def _(pe):
            def project_k(at, c):
                wait(pe, ctx_loaded, at.count(c, 16))
                wait(pe, v_ready, at.count(c - 1))
                pe.matmul(bank_b[:, 0:S], wk[:, :], ctx_t[:, at.stage(c)], start=True, stop=True).then_inc(k_proj, 1)

            def turn_xn(at, c):
                wait(pe, xn_done[0], at.count(c))
                wait(pe, k_rest_done, at.count(c))
                for t in range(TT):
                    mm = pe.transpose(bank_b[:, t * P:(t + 1) * P], xn[:, 0, t], ident[:, :])
                mm.then_inc(xn_turned[0], 1)

            def project_q(at, c):
                wait(pe, xn_t_ready[0], at.count(c))
                pe.matmul(bank_b[:, 0:S], wq[:, :], xn_t[:, 0], start=True, stop=True).then_inc(q_proj, 1)

            def project_v(at, c):
                wait(pe, q_rest_done, at.count(c))
                for t in range(TT):
                    mm = pe.matmul(bank_b[:, t * P:(t + 1) * P], ctx_t[:, at.stage(c), t * P:(t + 1) * P], wv[:, :],
                                   start=True, stop=True)
                mm.then_inc(v_proj, 1)

            def max_scores(at, c, k):
                if k == 0:
                    wait(pe, k_spread, at.count(c, K_SPREAD))
                    wait(pe, q_spread, at.count(c, Q_SPREAD))
                if k >= 2:
                    wait(pe, max_done[k - 2], at.count(c))
                else:
                    wait(pe, max_done[k + HEADS - 2], at.count(c - 1))
                for t in range(TT):
                    mm = pe.matmul(max_bank[k % 2][:, t * S:(t + 1) * S],
                                   q_ops[at.stage(c)][0:MAX_ROWS, k, t * P:(t + 1) * P],
                                   k_ops[at.stage(c)][0:MAX_ROWS, k, :], start=True, stop=True)
                mm.then_inc(max_scores_ready[k], 1)

            def turn_max(at, c, g):
                wait(pe, max_part2[g], at.count(c))
                if g == 1:
                    wait(pe, max_t_ready[0], at.count(c))
                turned = bank_a[:, :].bitcast(BF16)
                for t in range(TT):
                    mm = pe.transpose(turned[0:2 * HALF, t * P:(t + 1) * P],
                                      max_parts[:, g, t].rearrange("p i h -> p (i h)"), ident_bf[:, :])
                mm.then_inc(max_turned[g], 1)

            def scores(at, k):
                if k % HALF == 0:
                    wait(pe, shift_spread[k // HALF], at.count(0, 16))
                if k >= 2:
                    wait(pe, probs_ready[k - 2], at.count(0))
                else:
                    wait(pe, probs_ready[k + HEADS - 2], at.count(-1))
                for t in range(TT):
                    mm = pe.matmul(score_bank[k % 2][:, t * S:(t + 1) * S],
                                   k_ops[at.stage(0)][0:ROWS, k, t * P:(t + 1) * P],
                                   q_ops[at.stage(0)][0:ROWS, k, :], start=True, stop=True)
                mm.then_inc(scores_ready[k], 1)

            def times_v(at, c, quad):
                wait(pe, probs_ready[LANES * quad + LANES - 1], at.count(c))
                g, first = quad // 2, quad % 2 == 0
                if quad == 0:
                    wait(pe, v_ready, at.count(c))
                if first:
                    wait(pe, pv_copied[g], at.count(c - 1))
                for t in range(TT):
                    for lane in range(LANES):
                        k = LANES * quad + lane
                        mm = pe.matmul(pv_bank[g][VCOLS * lane:VCOLS * (lane + 1), 0:S],
                                       v_ops[at.stage(c)][:, t, k, :], probs[:, k % RING, t],
                                       start=first and t == 0, stop=not first and t == TT - 1)
                mm.then_inc(pv_done[quad], 1)

            def turn_pv(at):
                wait(pe, pv_copied[1], at.count(-1))
                for t in range(TT):
                    for g in range(2):
                        n = 2 * t + g
                        mm = pe.transpose(bank_a[:, n * P:(n + 1) * P], pv_t[:, g, t * P:(t + 1) * P], ident[:, :])
                mm.then_inc(pv_turned, 1)

            def turn_attn(at):
                wait(pe, attn_done, at.count(-1))
                for t in range(TT):
                    mm = pe.transpose(bank_a[:, t * P:(t + 1) * P],
                                      attn[:, 2 * t:2 * t + 2].rearrange("p g s l d -> p (g s l d)"), ident[:, :])
                mm.then_inc(attn_turned, 1)

            def project_attn(at):
                wait(pe, attn_t_ready, at.count(-1))
                for t in range(TT):
                    mm = pe.matmul(bank_a[:, t * P:(t + 1) * P], attn_t[:, t * P:(t + 1) * P], wo[:, :],
                                   start=True, stop=True)
                mm.then_inc(attn_proj, 1)

            def turn_xn2(at):
                wait(pe, xn_done[1], at.count(-1))
                for t in range(TT):
                    mm = pe.transpose(bank_b[:, t * P:(t + 1) * P], xn[:, 1, t], ident[:, :])
                mm.then_inc(xn_turned[1], 1)

            def project_gate_up(at, n):
                if n == 0:
                    wait(pe, xn_t_ready[1], at.count(-1))
                if n == 2:
                    wait(pe, hidden_done[0], at.count(-1))
                to = (bank_a, bank_b)[n % 2]
                for i in range(2):
                    mm = pe.matmul(to[:, i * S:(i + 1) * S], wgu[:, n, i], xn_t[:, 1], start=True, stop=True)
                mm.then_inc(gate_up[n], 1)

            def project_down(at):
                wait(pe, hidden_done[CH - 1], at.count(-1))
                for t in range(TT):
                    for n in range(CH):
                        mm = pe.matmul(bank_b[:, t * P:(t + 1) * P], hidden[:, n, t * P:(t + 1) * P], wd[:, n],
                                       start=n == 0, stop=n == CH - 1)
                mm.then_inc(down_proj, 1)

            start = Step(0, 0)
            pe.wait_ge(wk_in, 16)
            project_k(start, 0)
            pe.wait_ge(ident_ready, 2)
            turn_xn(start, 0)
            pe.wait_ge(wq_in, 16)
            project_q(start, 0)
            pe.wait_ge(wv_in, 16)
            project_v(start, 0)
            project_k(start, 1)
            turn_xn(start, 1)
            project_q(start, 1)
            project_v(start, 1)
            for k in range(HEADS):
                max_scores(start, 0, k)
                if k == HALF + 1:
                    turn_max(start, 0, 0)
            pe.wait_ge(wo_in, 16)
            pe.wait_ge(weights_ready, 2)

            def step(at, before, now, ahead, next2):
                for k in range(HEADS):
                    if now:
                        scores(at, k)
                    if ahead:
                        max_scores(at, 1, k)
                    if k == 0 and now:
                        turn_max(at, 0, 1)
                    if k == 1 and before:
                        times_v(at, -1, 3)
                    if k == 2 and next2:
                        project_k(at, 2)
                    if k == 3 and before:
                        wait(pe, max_t_ready[1], at.count(0 if now else -1))
                        turn_pv(at)
                    if k == 3 and next2:
                        turn_xn(at, 2)
                    if k == 5 and before:
                        turn_attn(at)
                    if k == 5 and now:
                        times_v(at, 0, 0)
                    if k == 5 and next2:
                        project_q(at, 2)
                    if k == 6 and before:
                        project_attn(at)
                    if k == 7 and next2:
                        project_v(at, 2)
                    if k == 9 and now:
                        times_v(at, 0, 1)
                    if k == 9 and ahead:
                        wait(pe, max_t_ready[1], at.count(0))
                        if before:
                            wait(pe, x1_done, at.count(-1))
                        turn_max(at, 1, 0)
                    if k == 10 and before:
                        if next2:
                            wait(pe, v_ready, at.count(2))
                        turn_xn2(at)
                    if k == 11 and before:
                        if ahead:
                            wait(pe, max_t_ready[0], at.count(1))
                        project_gate_up(at, 0)
                    if k == 12 and before:
                        project_gate_up(at, 1)
                    if k == 13 and before:
                        project_gate_up(at, 2)
                    if k == 13 and now:
                        times_v(at, 0, 2)
                    if k == 15 and before:
                        project_down(at)

            steps(pe, step, 1, 16, K_SPREAD, Q_SPREAD)

        @block.scalar
        def _(act):
            def part1_k(at, c):
                wait(act, k_proj, at.count(c))
                wait(act, k_spread, at.count(c - 1, K_SPREAD))
                act.activation(k_parts[:, 0], bank_b[:, 0:S], ACT.Copy).then_inc(k_part1, 1)

            def part2_k(at, c):
                wait(act, k_rest_done, at.count(c))
                act.activation(k_parts[:, 1], k_rest[:, :], ACT.Copy).then_inc(k_part2, 1)

            def copy_xn_t(at, c, norm):
                wait(act, xn_turned[norm], at.count(c))
                act.activation(xn_t[:, norm], bank_b[:, 0:S], ACT.Copy).then_inc(xn_t_ready[norm], 1)

            def part1_q(at, c):
                wait(act, q_proj, at.count(c))
                wait(act, q_spread, at.count(c - 1, Q_SPREAD))
                act.activation(q_parts[:, 0], bank_b[:, 0:S], ACT.Copy).then_inc(q_part1, 1)

            def part2_q(at, c):
                wait(act, q_rest_done, at.count(c))
                act.activation(q_parts[:, 1], q_rest[:, :], ACT.Copy).then_inc(q_part2, 1)

            def place_v(at, c):
                wait(act, v_proj, at.count(c))
                wait(act, pv_done[3], at.count(c - STAGES))
                to = v_ops[at.stage(c)][:, :, :, :].rearrange("p t (g s l) c -> p (t g) s l c", g=2, s=2)
                of = bank_b[:, 0:TT * D].rearrange("p (n s l d) -> p n s l d", s=2, l=LANES, d=DK)
                for s in range(2):
                    ins = act.activation(to[:, :, s, :, DK * s:DK * (s + 1)], of[:, :, s], ACT.Copy)
                ins.then_inc(v_ready, 1)

            def copy_max_t(at, c, g):
                wait(act, max_turned[g], at.count(c))
                act.activation(max_t[g][:, :], bank_a[:, :].bitcast(BF16)[0:2 * HALF, 0:S], ACT.Copy)\
                    .then_inc(max_t_ready[g], 1)

            def exp(at, k):
                if k % LANES == 0:
                    quad = k // LANES
                    if quad >= 2:
                        wait(act, pv_done[quad - 2], at.count(0))
                    else:
                        wait(act, pv_done[quad + 2], at.count(-1))
                wait(act, scores_ready[k], at.count(0))
                act.activation(probs[:, k % RING].rearrange("p t s -> p (t s)"), score_bank[k % 2][:, :], ACT.Exp,
                               scale=SCALE).then_inc(probs_ready[k], 1)

            def copy_pv(at, c, g):
                wait(act, pv_done[2 * g + 1], at.count(c))
                act.activation(pv_t[:, g], pv_bank[g][:, 0:S], ACT.Copy).then_inc(pv_copied[g], 1)

            def copy_attn_t(at):
                wait(act, attn_turned, at.count(-1))
                act.activation(attn_t[:, :], bank_a[:, 0:S], ACT.Copy).then_inc(attn_t_ready, 1)

            def gate_tanh(at, n):
                wait(act, gate_up[n], at.count(-1))
                act.activation(tanh[:, n % 2], (bank_a, bank_b)[n % 2][:, 0:S], ACT.Tanh, scale=0.5 * WEIGHT_SCALE)\
                    .then_inc(tanh_ready[n], 1)

            act.dma_start(wk[:, :], wkT).then_inc(wk_in, 16)
            act.dma_start(wq[:, :], wqT).then_inc(wq_in, 16)
            act.dma_start(wv[:, :], wvT).then_inc(wv_in, 16)
            start = Step(0, 0)
            part1_k(start, 0)
            part2_k(start, 0)
            copy_xn_t(start, 0, 0)
            part1_q(start, 0)
            part2_q(start, 0)
            act.wait_ge(v_filled, 3 * STAGES)
            place_v(start, 0)
            act.wait_ge(wgu_in, 16)
            act.activation(wgu[:, :, :, :], wgu_int[:, :, :, :], ACT.Copy).then_inc(weights_ready, 1)
            act.wait_ge(wd_in, 16)
            act.activation(wd[:, :, :], wd_int[:, :, :], ACT.Copy).then_inc(weights_ready, 1)
            part1_k(start, 1)
            part2_k(start, 1)
            copy_xn_t(start, 1, 0)
            part1_q(start, 1)
            part2_q(start, 1)
            place_v(start, 1)
            copy_max_t(start, 0, 0)

            def step(at, before, now, ahead, next2):
                for k in range(HEADS):
                    if now:
                        exp(at, k)
                    if k == 1 and now:
                        copy_max_t(at, 0, 1)
                    if k == 2 and before:
                        copy_pv(at, -1, 1)
                    if k == 2 and next2:
                        part1_k(at, 2)
                    if k == 3 and next2:
                        part2_k(at, 2)
                    if k == 4 and next2:
                        copy_xn_t(at, 2, 0)
                    if k == 5 and next2:
                        part1_q(at, 2)
                    if k == 6 and before:
                        copy_attn_t(at)
                    if k == 6 and next2:
                        part2_q(at, 2)
                    if k == 8 and next2:
                        place_v(at, 2)
                    if k == 10 and ahead:
                        copy_max_t(at, 1, 0)
                    if k == 10 and now:
                        copy_pv(at, 0, 0)
                    if k == 11 and before:
                        copy_xn_t(at, -1, 1)
                    if k == 12 and before:
                        gate_tanh(at, 0)
                    if k == 13 and before:
                        gate_tanh(at, 1)
                    if k == 14 and before:
                        gate_tanh(at, 2)

            steps(act, step, 1, K_SPREAD, Q_SPREAD)

        @block.vector
        def _(dve):
            def norm_stats(at, c, norm):
                if norm == 0:
                    wait(dve, x_loaded, at.count(c, 16))
                else:
                    wait(dve, x1_done, at.count(c))
                for t in range(TT):
                    of = x_in[:, at.stage(c), t] if norm == 0 else x1[:, t]
                    ins = dve.bn_stats(stats[:, norm, t], of)
                ins.then_inc(stats_done[norm], 1)

            def norm_moments(at, c, norm):
                settle(dve)
                wait(dve, stats_done[norm], at.count(c))
                wait(dve, shift_done[norm], at.count(c - 1) if norm == 0 else 0)
                for t in range(TT):
                    ins = dve.bn_aggr(moments[:, norm, t], stats[:, norm, t])
                ins.then_inc(moments_done[norm], 1)

            def rest_k(at, c):
                wait(dve, k_part1, at.count(c))
                dve.tensor_tensor(k_rest[:, :], bank_b[:, 0:S], k_parts[:, 0], ALU.subtract).then_inc(k_rest_done, 1)

            def rest_q(at, c):
                wait(dve, q_part1, at.count(c))
                dve.tensor_tensor(q_rest[:, :], bank_b[:, 0:S], q_parts[:, 0], ALU.subtract).then_inc(q_rest_done, 1)

            def head_max(at, c, k):
                wait(dve, max_scores_ready[k], at.count(c))
                dve.tensor_reduce(neg_max[:, k // HALF, :, k % HALF],
                                  max_bank[k % 2][:, :].rearrange("p (t s) -> p t s", t=TT), AX.X, ALU.max,
                                  negate=True).then_inc(max_done[k], 1)

            def part1_max(at, c, g):
                wait(dve, max_done[HALF * g + HALF - 1], at.count(c))
                dve.tensor_copy(max_parts[:, g, :, 0], neg_max[:, g]).then_inc(max_part1[g], 1)

            def part2_max(at, c, g):
                wait(dve, max_part1[g], at.count(c))
                dve.tensor_tensor(max_parts[:, g, :, 1], neg_max[:, g], max_parts[:, g, :, 0], ALU.subtract)\
                    .then_inc(max_part2[g], 1)

            turned = bank_a[:, :].rearrange("p (n l c) -> p n l c", l=LANES, c=VCOLS)

            def reciprocals(at):
                wait(dve, pv_turned, at.count(-1))
                dve.reciprocal(recip[:, :, :, :], turned[:, :, :, 2 * DK:2 * DK + 2]).then_inc(recip_done, 1)

            def normalise(at):
                wait(dve, recip_done, at.count(-1))
                for s in range(2):
                    ins = dve.tensor_tensor(attn[:, :, s], turned[:, :, :, DK * s:DK * (s + 1)],
                                            recip[:, :, :, s:s + 1].broadcast_to([P, 2 * TT, LANES, DK]), ALU.mult)
                ins.then_inc(attn_done, 1)

            def residual(at):
                wait(dve, attn_proj, at.count(-1))
                wait(dve, res_loaded, at.count(-1, 16))
                dve.tensor_tensor(x1[:, :, :], bank_a[:, 0:TT * D].rearrange("p (t d) -> p t d", t=TT),
                                  x_res[:, at.stage(-1)], ALU.add).then_inc(x1_done, 1)

            def gate(at, n):
                both = (bank_a, bank_b)[n % 2]
                wait(dve, tanh_ready[n], at.count(-1))
                dve.scalar_tensor_tensor(out=gated[:, n % 2], in0=tanh[:, n % 2], scalar=1.0, in1=both[:, 0:S],
                                         op0=ALU.add, op1=ALU.mult).then_inc(gated_done[n], 1)

            def times_up(at, n):
                both = (bank_a, bank_b)[n % 2]
                wait(dve, gated_done[n], at.count(-1))
                dve.tensor_tensor(hidden[:, n], both[:, S:2 * S], gated[:, n % 2], ALU.mult)\
                    .then_inc(hidden_done[n], 1)

            def output(at, last):
                if last:
                    wait(dve, stored, at.count(-2, 16))
                wait(dve, down_proj, at.count(-1))
                dve.scalar_tensor_tensor(out=y[:, :, :], in0=bank_b[:, 0:TT * D].rearrange("p (t d) -> p t d", t=TT),
                                         scalar=0.5 * WEIGHT_SCALE**3, in1=x1[:, :, :],
                                         op0=ALU.mult, op1=ALU.add).then_inc(y_done, 1)

            def fill_k(i):
                for rows, value in ((slice(0, MAX_ROWS), 0.0), (slice(SHIFT_ROW, ROWS), ONES_PAIR)):
                    dve.memset(k_ops[i][rows].rearrange("p h s -> p (h s)").bitcast(F32), value)\
                        .then_inc(ops_filled[i], 1)

            start = Step(0, 0)
            fill_k(0)
            norm_stats(start, 0, 0)
            norm_moments(start, 0, 0)
            dve.wait_ge(mask_in, 16)
            dve.tensor_scalar(mask_f[:, :], mask_u8[:, :], -1.0, 3e38, ALU.add, ALU.mult).then_inc(mask_sub, 1)
            rest_k(start, 0)
            dve.wait_ge(mask_sub, 1)
            dve.tensor_scalar(mask_bias[:, :], mask_f[:, :], 1e3, None, ALU.mult).then_inc(mask_ready, 1)
            rest_q(start, 0)
            norm_stats(start, 1, 0)
            norm_moments(start, 1, 0)
            rest_k(start, 1)
            rest_q(start, 1)
            for i in range(1, STAGES):
                fill_k(i)
            for k in range(HEADS):
                head_max(start, 0, k)
                if k == HALF:
                    part1_max(start, 0, 0)
                if k == HALF + 1:
                    part2_max(start, 0, 0)

            def step(at, before, now, ahead, next2):
                for k in range(HEADS):
                    if ahead:
                        head_max(at, 1, k)
                    if k == 0 and now:
                        part1_max(at, 0, 1)
                    if k == 0 and next2:
                        norm_stats(at, 2, 0)
                    if k == 0 and now:
                        part2_max(at, 0, 1)
                    if k == 0 and next2:
                        norm_moments(at, 2, 0)
                    if k == 2 and next2:
                        rest_k(at, 2)
                    if k == 4 and before:
                        reciprocals(at)
                    if k == 5 and before:
                        normalise(at)
                    if k == 6 and next2:
                        rest_q(at, 2)
                    if k == 7 and before:
                        residual(at)
                        norm_stats(at, -1, 1)
                        norm_moments(at, -1, 1)
                    if k == 8 and ahead:
                        part1_max(at, 1, 0)
                    if k == 9 and ahead:
                        part2_max(at, 1, 0)
                    if k == 12 and before:
                        gate(at, 0)
                    if k == 13 and before:
                        times_up(at, 0)
                        gate(at, 1)
                    if k == 14 and before:
                        times_up(at, 1)
                        gate(at, 2)
                    if k == 15 and before:
                        times_up(at, 2)
                        output(at, not now)

            steps(dve, step, 1, 16)

        @block.gpsimd
        def _(pool):
            def normalise(at, c, norm):
                settle(pool)
                wait(pool, moments_done[norm], at.count(c))
                pool.tensor_scalar(var_eps[:, norm], moments[:, norm, :, 1], 1.0, EPS, ALU.mult, ALU.add)\
                    .then_inc(var_done[norm], 1)
                wait(pool, var_done[norm], at.count(c))
                pool.tensor_tensor(rstd[:, norm], var_eps[:, norm], minus_half[:, :], ALU.pow)\
                    .then_inc(rstd_done[norm], 1)
                settle(pool)
                wait(pool, rstd_done[norm], at.count(c))
                for t in range(TT):
                    ins = pool.tensor_scalar(shift[:, norm, t:t + 1], moments[:, norm, t, 0:1],
                                             rstd[:, norm, t:t + 1], -1.0, ALU.mult, ALU.mult)
                ins.then_inc(shift_done[norm], 1)
                settle(pool)
                wait(pool, shift_done[norm], at.count(c))
                if norm == 0:
                    wait(pool, xn_turned[0], at.count(c - 1))
                for t in range(TT):
                    of = x_in[:, at.stage(c), t] if norm == 0 else x1[:, t]
                    ins = pool.tensor_scalar(xn[:, norm, t], of, rstd[:, norm, t:t + 1], shift[:, norm, t:t + 1],
                                             ALU.mult, ALU.add)
                ins.then_inc(xn_done[norm], 1)

            def last_part_k(at, c):
                wait(pool, k_part2, at.count(c))
                pool.tensor_tensor(k_parts[:, 2], k_rest[:, :], k_parts[:, 1], ALU.subtract).then_inc(k_part3, 1)

            def last_part_q(at, c):
                wait(pool, q_part2, at.count(c))
                pool.tensor_tensor(q_parts[:, 2], q_rest[:, :], q_parts[:, 1], ALU.subtract).then_inc(q_part3, 1)

            def fill_q(i):
                pool.memset(q_ops[i][0:MAX_ROWS].rearrange("p h s -> p (h s)").bitcast(F32), ONES_PAIR)\
                    .then_inc(ops_filled[i], 1)

            pool.memset(minus_half[:, :], -0.5).then_inc(consts_ready, 1)
            pool.memset(ident[:, :], 0.0).then_inc(ident_zero, 1)
            pool.memset(ident_bf[:, :], 0.0).then_inc(ident_zero, 1)
            pool.wait_ge(ident_zero, 2)
            for m in (ident, ident_bf):
                pool.affine_select(out=m[:, :], in_=m[:, :], compare_op=ALU.not_equal, fill=1.0, base=0,
                                   pattern=[[-1, P]], channel_multiplier=1).then_inc(ident_ready, 1)
            start = Step(0, 0)
            pool.wait_ge(consts_ready, 1)
            normalise(start, 0, 0)
            last_part_k(start, 0)
            fill_q(0)
            last_part_q(start, 0)
            for i in range(STAGES):
                pool.memset(v_ops[i][:, :, :, :], 0.0).then_inc(v_zero, 1)
                pool.wait_ge(v_zero, i + 1)
                for s in range(2):
                    to = v_ops[i][:, :, :, :].rearrange("p t (g s l) c -> p (t g) s l c", g=2, s=2)
                    pool.memset(to[:, :, s, :, 2 * DK + s:2 * DK + s + 1], 1.0).then_inc(v_filled, 1)
                pool.memset(minus_half[:, :], -0.5).then_inc(v_filled, 1)
            normalise(start, 1, 0)
            last_part_k(start, 1)
            last_part_q(start, 1)
            for i in range(1, STAGES):
                fill_q(i)

            def step(at, before, now, ahead, next2):
                if next2:
                    normalise(at, 2, 0)
                    last_part_k(at, 2)
                    last_part_q(at, 2)
                if before:
                    normalise(at, -1, 1)

            steps(pool, step, 1)


INPUTS = ("x", "ctxT", "mask", "wqT", "wkT", "wvT", "woT", "wguT", "wdT")


def kernel(x, ctx_1024, mask_BxS2_bf1, L0_xattn_w_q, L0_xattn_w_k, L0_xattn_w_v, L0_xattn_w_o, L0_ffn_w_gate,
           L0_ffn_w_up, L0_ffn_w_down):
    import concourse.bacc as bacc
    import numpy as np
    from concourse.bass_utils import run_bass_kernel_spmd

    def by_place(w):
        w = np.asarray(w)
        return w.reshape(HEADS, DK, w.shape[1]).transpose(2, 1, 0).reshape(w.shape[1], HEADS * DK)

    ctx = np.asarray(ctx_1024)
    gate, up, down = (np.asarray(w) for w in (L0_ffn_w_gate, L0_ffn_w_up, L0_ffn_w_down))
    chunks = gate.shape[0] // P
    arrays = {
        "x": np.asarray(x),
        "ctxT": ctx.transpose(0, 2, 1),
        "mask": np.asarray(mask_BxS2_bf1).view(np.uint8),
        "wqT": by_place(L0_xattn_w_q),
        "wkT": by_place(L0_xattn_w_k),
        "wvT": np.asarray(L0_xattn_w_v).T,
        "woT": np.asarray(L0_xattn_w_o).T,
        "wguT": np.stack([gate, up]).reshape(2, chunks, P, -1).transpose(3, 1, 0, 2),
        "wdT": down.reshape(-1, chunks, P).transpose(2, 1, 0),
    }
    arrays = {name: np.ascontiguousarray(a) for name, a in arrays.items()}
    nc = bacc.Bacc("TRN2", target_bir_lowering=False, num_devices=1)
    aps = [nc.dram_tensor(name, arrays[name].shape, mybir.dt.from_np(arrays[name].dtype), kind="ExternalInput").ap()
           for name in INPUTS]
    out = nc.dram_tensor("out", arrays["x"].shape, F32, kind="ExternalOutput").ap()
    build(nc, *aps, out)
    r = run_bass_kernel_spmd(nc, [arrays], core_ids=[0])
    return r.results[0]["out"]
```

```python
from contextlib import ExitStack

import concourse.bass as bass
from concourse import mybir

F32 = mybir.dt.float32
BF16 = mybir.dt.bfloat16
I32 = mybir.dt.int32
U8 = mybir.dt.uint8
ALU = mybir.AluOpType
ACT = mybir.ActivationFunctionType
AX = mybir.AxisListType

P = 128
HEADS = 16
DK = 8
PARTS = 3
PAIRS = ((0, 0), (0, 1), (0, 2), (1, 0), (1, 1), (2, 0))
MASK_ROW = DK * len(PAIRS)
MAX_ROWS = 96
SHIFT_ROW = 96
ROWS = SHIFT_ROW + 2
STAGES = 3
RING = 8
LANES = 4
VCOLS = 32
WEIGHT_SCALE = 1.0 / 127.0
EPS = 1e-5
ONES_PAIR = 1.0 + 0x3F80 / 2.0**23


class Step:

    def __init__(self, base, u, registers=None):
        self.base, self.u, self.registers = base, u, registers

    def count(self, c, unit=1):
        n = self.u + c + 1
        return (self.base + n) * unit if self.registers is None else self.registers[n, unit]

    def stage(self, c):
        return ((self.base if self.registers is None else 1) + self.u + c) % STAGES


def build(nc, x, ctxT, mask, wqT, wkT, wvT, woT, wguT, wdT, out):
    B, S, D = x.shape
    TT = S // P
    HALF = HEADS // 2
    CH = wdT.shape[1]
    SCALE = float(DK) ** -0.5

    with ExitStack() as ctx:
        def sb(name, shape, dt):
            return ctx.enter_context(nc.sbuf_tensor(name, shape, dt))

        def bank(name):
            return ctx.enter_context(nc.psum_tensor(name, [P, 512], F32))

        def sem(name):
            return ctx.enter_context(nc.semaphore(name))

        score_bank = [bank(f"score_bank{i}") for i in range(2)]
        max_bank = [bank(f"max_bank{i}") for i in range(2)]
        pv_bank = [bank(f"pv_bank{i}") for i in range(2)]
        bank_a, bank_b = bank("bank_a"), bank("bank_b")
        proj_bank = (bank_b, bank_a, bank_b)
        post_bank = pv_bank[1]
        chunk_bank = (pv_bank[0], bank_a, bank_b)

        ident = sb("ident", [P, P], F32)
        ident_bf = sb("ident_bf", [P, P], BF16)
        wq = sb("wq", [P, D], F32)
        wk = sb("wk", [P, D], F32)
        wv = sb("wv", [P, D], F32)
        wo = sb("wo", [P, D], F32)
        wgu_int = sb("wgu_int", [P, CH, 2, P], I32)
        wd_int = sb("wd_int", [P, CH, D], I32)
        wgu = sb("wgu", [P, CH, 2, P], F32)
        wd = sb("wd", [P, CH, D], F32)
        minus_half = sb("minus_half", [P, TT], F32)
        mask_u8 = sb("mask_u8", [B, S], U8)
        mask_f = sb("mask_f", [B, S], F32)
        mask_bias = sb("mask_bias", [B, S], BF16)
        mask_row = sb("mask_row", [1, B * S], BF16)
        x_in = sb("x_in", [P, STAGES, TT, D], F32)
        x_res = sb("x_res", [P, STAGES, TT, D], F32)
        ctx_t = sb("ctx_t", [P, STAGES, S], F32)
        q_ops = [sb(f"q_ops{i}", [P, HEADS, S], BF16) for i in range(STAGES)]
        k_ops = [sb(f"k_ops{i}", [P, HEADS, S], BF16) for i in range(STAGES)]
        v_ops = [sb(f"v_ops{i}", [P, TT, HEADS, VCOLS], F32) for i in range(STAGES)]
        k_parts = sb("k_parts", [P, STAGES, PARTS, S], BF16)
        q_parts = sb("q_parts", [P, STAGES, PARTS, S], BF16)
        k_rest = sb("k_rest", [P, S], F32)
        q_rest = sb("q_rest", [P, S], F32)
        stats = sb("stats", [P, 2, TT, 6], F32)
        moments = sb("moments", [P, 2, TT, 2], F32)
        var_eps = sb("var_eps", [P, 2, TT], F32)
        rstd = sb("rstd", [P, 2, TT], F32)
        xn = sb("xn", [P, 2, TT, D], F32)
        xn_t = sb("xn_t", [P, 2, S], F32)
        neg_max = sb("neg_max", [P, 2, TT, HALF], F32)
        max_parts = sb("max_parts", [P, 2, TT, 2, HALF], BF16)
        max_t = [sb(f"max_t{g}", [2 * HALF, S], BF16) for g in range(2)]
        probs = sb("probs", [P, RING, TT, S], F32)
        pv_t = sb("pv_t", [P, 2, S], F32)
        recip = sb("recip", [P, 2 * TT, LANES, 2], F32)
        attn = sb("attn", [P, 2 * TT, 2, LANES, DK], F32)
        attn_t = sb("attn_t", [P, S], F32)
        x1 = sb("x1", [P, STAGES, TT, D], F32)
        tanh = sb("tanh", [P, CH, S], F32)
        gated = sb("gated", [P, CH, S], F32)
        hidden = sb("hidden", [P, CH, S], F32)
        y = sb("y", [P, STAGES, TT, D], F32)

        wk_in, wq_in, wv_in, wo_in, wgu_in, wd_in = (sem(f"{w}_in") for w in ("wk", "wq", "wv", "wo", "wgu", "wd"))
        mask_in, mask_row_in = sem("mask_in"), sem("mask_row_in")
        x_loaded, ctx_loaded, res_loaded = sem("x_loaded"), sem("ctx_loaded"), sem("res_loaded")
        k_spread, q_spread = sem("k_spread"), sem("q_spread")
        shift_spread = [sem(f"shift_spread{g}") for g in range(2)]
        stored = sem("stored")
        K_SPREAD, Q_SPREAD = 16 * (len(PAIRS) + 1), 16 * len(PAIRS)
        ident_zero, ident_ready = sem("ident_zero"), sem("ident_ready")
        ops_filled = [sem(f"ops_filled{i}") for i in range(STAGES)]
        k_filled, table_loaded = sem("k_filled"), sem("table_loaded")
        v_zero, v_filled, consts_ready = sem("v_zero"), sem("v_filled"), sem("consts_ready")
        mask_sub, mask_ready = sem("mask_sub"), sem("mask_ready")
        weights_ready = sem("weights_ready")
        scores_ready = [sem(f"scores_ready{k}") for k in range(HEADS)]
        max_scores_ready = [sem(f"max_scores_ready{k}") for k in range(HEADS)]
        pv_done = [sem(f"pv_done{q}") for q in range(HEADS // LANES)]
        k_proj, v_proj, q_proj = sem("k_proj"), sem("v_proj"), sem("q_proj")
        xn_turned = [sem("xn1_turned"), sem("xn2_turned")]
        pv_turned, attn_turned, attn_proj = sem("pv_turned"), sem("attn_turned"), sem("attn_proj")
        max_turned = [sem(f"max_turned{g}") for g in range(2)]
        gate_up = [sem(f"gate_up{c}") for c in range(CH)]
        down_proj = sem("down_proj")
        probs_ready = [sem(f"probs_ready{k}") for k in range(HEADS)]
        k_part1, k_part2, q_part1, q_part2 = sem("k_part1"), sem("k_part2"), sem("q_part1"), sem("q_part2")
        v_ready = sem("v_ready")
        xn_t_ready = [sem("xn1_t_ready"), sem("xn2_t_ready")]
        pv_copied = [sem(f"pv_copied{g}") for g in range(2)]
        attn_t_ready = sem("attn_t_ready")
        max_t_ready = [sem(f"max_t_ready{g}") for g in range(2)]
        tanh_ready = [sem(f"tanh_ready{c}") for c in range(CH)]
        max_done = [sem(f"max_done{k}") for k in range(HEADS)]
        stats_done = [sem("stats1_done"), sem("stats2_done")]
        moments_done = [sem("moments1_done"), sem("moments2_done")]
        k_rest_done, q_rest_done = sem("k_rest_done"), sem("q_rest_done")
        max_part1 = [sem(f"max_part1_{g}") for g in range(2)]
        max_part2 = [sem(f"max_part2_{g}") for g in range(2)]
        recip_done, attn_done, x1_done = sem("recip_done"), sem("attn_done"), sem("x1_done")
        gated_done = [sem(f"gated_done{c}") for c in range(CH)]
        hidden_done = [sem(f"hidden_done{c}") for c in range(CH)]
        y_done = sem("y_done")
        var_done = [sem("var1_done"), sem("var2_done")]
        rstd_done = [sem("rstd1_done"), sem("rstd2_done")]
        xn_done = [sem("xn1_done"), sem("xn2_done")]
        k_part3, q_part3 = sem("k_part3"), sem("q_part3")

        block = ctx.enter_context(nc.Block())

        def wait(eng, s, n):
            if not isinstance(n, int) or n > 0:
                eng.wait_ge(s, n)

        def settle(eng):
            eng.wait_ge(consts_ready, 1)

        def steps(eng, step, last_heads, finish, *units):
            step(Step(0, 0), False)
            with eng.Fori(0, (B - 2) // STAGES) as i:
                registers = {(n, unit): eng.snap((i * STAGES + 1 + n) * unit)
                             for unit in units for n in range(STAGES + 3)}
                for value in registers.values():
                    eng.to_reg(value)
                for u in range(STAGES):
                    step(Step(i * STAGES + 1, u, registers), True)
            last_heads(Step(B - 1, 0))
            finish(Step(B, 0), Step(B - 1, 0))


        @block.sync
        def _(sp):
            def load(at, c):
                b = at.base + at.u + c
                b = b if isinstance(b, int) else b & (B - 1)
                settle(sp)
                wait(sp, x_loaded, at.count(c - 1, 16))
                wait(sp, xn_done[0], at.count(c - STAGES))
                sp.dma_start(x_in[:, at.stage(c)], x[b].rearrange("(t p) d -> p t d", p=P)).then_inc(x_loaded, 16)
                settle(sp)
                wait(sp, ctx_loaded, at.count(c - 1, 16))
                wait(sp, v_proj, at.count(c - STAGES))
                sp.dma_start(ctx_t[:, at.stage(c)], ctxT[b]).then_inc(ctx_loaded, 16)

            def spread_parts(at, c, side, parts):
                ready = ((q_part1, q_part2, q_part3), (k_part1, k_part2, k_part3))[side]
                ops, of, landed = ((q_ops, q_parts, q_spread), (k_ops, k_parts, k_spread))[side]
                for part in parts:
                    settle(sp)
                    wait(sp, ready[part], at.count(c))
                    for n, pair in enumerate(PAIRS):
                        if pair[side] == part:
                            sp.dma_start(ops[at.stage(c)][DK * n:DK * (n + 1)], of[:, at.stage(c), part])\
                                .then_inc(landed, 16)

            def spread_k(at, c):
                b = at.base + at.u + c
                b = b if isinstance(b, int) else b & (B - 1)
                ops = k_ops[at.stage(c)]
                settle(sp)
                wait(sp, k_spread, at.count(c - 1, K_SPREAD))
                wait(sp, scores_ready[HEADS - 1], at.count(c - STAGES))
                spread_parts(at, c, 1, range(PARTS))
                sp.dma_start(ops[MASK_ROW:MASK_ROW + 1],
                             mask_row[0:1, bass.ds(b * S, S)].rearrange("o (n s) -> o n s", n=1)
                             .broadcast_to([1, HEADS, S])).then_inc(k_spread, 16)

            def spread_q(at, c):
                settle(sp)
                wait(sp, q_spread, at.count(c - 1, Q_SPREAD))
                spread_parts(at, c, 0, range(PARTS))

            def spread_shift(at, c, g):
                wait(sp, max_t_ready[g], at.count(c))
                sp.dma_start(q_ops[at.stage(c)][SHIFT_ROW:ROWS, HALF * g:HALF * (g + 1)],
                             max_t[g][:, :]).then_inc(shift_spread[g], 16)

            def spread_mask(c):
                sp.dma_start(k_ops[c][MASK_ROW:MASK_ROW + 1],
                             mask_row[0:1, c * S:(c + 1) * S].rearrange("o (n s) -> o n s", n=1)
                             .broadcast_to([1, HEADS, S])).then_inc(k_spread, 16)

            start = Step(0, 0)
            sp.dma_start(ctx_t[:, 0], ctxT[0]).then_inc(ctx_loaded, 16)
            sp.dma_start(x_in[:, 0], x[0].rearrange("(t p) d -> p t d", p=P)).then_inc(x_loaded, 16)
            sp.dma_start(wv[:, :], wvT).then_inc(wv_in, 16)
            sp.dma_start(mask_u8[:, :], mask).then_inc(mask_in, 16)
            load(start, 1)
            sp.wait_ge(ops_filled[0], 2)
            spread_parts(start, 0, 1, (0, 1, 2))
            sp.wait_ge(mask_ready, 1)
            sp.dma_start(mask_row[0:1, :], mask_bias[:, :]).then_inc(mask_row_in, 16)
            spread_parts(start, 0, 0, (0,))
            sp.wait_ge(mask_row_in, 16)
            spread_mask(0)
            spread_parts(start, 0, 0, (1, 2))
            sp.wait_ge(ops_filled[1], 2)
            sp.wait_ge(k_spread, K_SPREAD)
            spread_parts(start, 1, 1, (0, 1, 2))
            spread_mask(1)
            sp.wait_ge(q_spread, Q_SPREAD)
            spread_parts(start, 1, 0, (0, 1, 2))
            load(start, 2)
            spread_shift(start, 0, 0)
            sp.dma_start(wo[:, :], woT).then_inc(wo_in, 16)
            sp.dma_start(wgu_int[:, :, :, :], wguT).then_inc(wgu_in, 16)
            sp.dma_start(wd_int[:, :, :], wdT).then_inc(wd_in, 16)
            sp.wait_ge(ops_filled[2], 2)

            def load_res(at):
                b = at.base + at.u
                settle(sp)
                wait(sp, res_loaded, at.count(-1, 16))
                sp.dma_start(x_res[:, at.stage(0)], x[b].rearrange("(t p) d -> p t d", p=P))\
                    .then_inc(res_loaded, 16)

            def store(at):
                b = at.base + at.u - 1
                settle(sp)
                wait(sp, y_done, at.count(-1))
                sp.dma_start(out[b].rearrange("(t p) d -> p t d", p=P), y[:, at.stage(-1)]).then_inc(stored, 16)
                settle(sp)
                wait(sp, stored, at.count(-1, 16))

            def step(at, before):
                load(at, 3)
                load_res(at)
                spread_shift(at, 0, 1)
                spread_k(at, 2)
                spread_q(at, 2)
                spread_shift(at, 1, 0)
                if before:
                    store(at)

            def last_heads(at):
                load_res(at)
                spread_shift(at, 0, 1)

            def finish(at, previous):
                store(previous)
                store(at)

            steps(sp, step, last_heads, finish, 1, 16, K_SPREAD, Q_SPREAD)
            sp.wait_ge(k_spread, (B + 1) * K_SPREAD)
            sp.wait_ge(q_spread, (B + 1) * Q_SPREAD)
            sp.wait_ge(x_loaded, (B + 2) * 16)
            sp.wait_ge(ctx_loaded, (B + 2) * 16)

        @block.tensor
        def _(pe):
            def project_k(at, c):
                wait(pe, ctx_loaded, at.count(c, 16))
                if c != 1:
                    wait(pe, v_ready, at.count(c - 1))
                pe.matmul(proj_bank[c][:, 0:S], wk[:, :], ctx_t[:, at.stage(c)], start=True, stop=True)\
                    .then_inc(k_proj, 1)

            def turn_xn(at, c):
                wait(pe, xn_done[0], at.count(c))
                wait(pe, k_rest_done, at.count(c))
                for t in range(TT):
                    mm = pe.transpose(proj_bank[c][:, t * P:(t + 1) * P], xn[:, 0, t], ident[:, :])
                mm.then_inc(xn_turned[0], 1)

            def project_q(at, c):
                wait(pe, xn_t_ready[0], at.count(c))
                pe.matmul(proj_bank[c][:, 0:S], wq[:, :], xn_t[:, 0], start=True, stop=True).then_inc(q_proj, 1)

            def project_v(at, c):
                wait(pe, q_rest_done, at.count(c))
                for t in range(TT):
                    mm = pe.matmul(proj_bank[c][:, t * P:(t + 1) * P], ctx_t[:, at.stage(c), t * P:(t + 1) * P],
                                   wv[:, :], start=True, stop=True)
                mm.then_inc(v_proj, 1)

            def max_scores(at, c, k):
                if k == 0:
                    wait(pe, k_spread, at.count(c, K_SPREAD))
                    wait(pe, q_spread, at.count(c, Q_SPREAD))
                if k >= 2:
                    wait(pe, max_done[k - 2], at.count(c))
                else:
                    wait(pe, max_done[k + HEADS - 2], at.count(c - 1))
                for t in range(TT):
                    mm = pe.matmul(max_bank[k % 2][:, t * S:(t + 1) * S],
                                   q_ops[at.stage(c)][0:MAX_ROWS, k, t * P:(t + 1) * P],
                                   k_ops[at.stage(c)][0:MAX_ROWS, k, :], start=True, stop=True)
                mm.then_inc(max_scores_ready[k], 1)

            def turn_max(at, c, g):
                wait(pe, max_part2[g], at.count(c))
                if g == 1:
                    wait(pe, max_t_ready[0], at.count(c))
                elif c == 1:
                    wait(pe, max_t_ready[1], at.count(c - 1))
                turned = bank_a[:, :].bitcast(BF16)
                for t in range(TT):
                    mm = pe.transpose(turned[0:2 * HALF, t * P:(t + 1) * P],
                                      max_parts[:, g, t].rearrange("p i h -> p (i h)"), ident_bf[:, :])
                mm.then_inc(max_turned[g], 1)

            def scores(at, k):
                if k % HALF == 0:
                    wait(pe, shift_spread[k // HALF], at.count(0, 16))
                if k >= 2:
                    wait(pe, probs_ready[k - 2], at.count(0))
                else:
                    wait(pe, probs_ready[k + HEADS - 2], at.count(-1))
                for t in range(TT):
                    mm = pe.matmul(score_bank[k % 2][:, t * S:(t + 1) * S],
                                   k_ops[at.stage(0)][0:ROWS, k, t * P:(t + 1) * P],
                                   q_ops[at.stage(0)][0:ROWS, k, :], start=True, stop=True)
                mm.then_inc(scores_ready[k], 1)

            def times_v(at, c, quad):
                wait(pe, probs_ready[LANES * quad + LANES - 1], at.count(c))
                g, first = quad // 2, quad % 2 == 0
                if quad == 0:
                    wait(pe, v_ready, at.count(c))
                if first:
                    wait(pe, pv_copied[g], at.count(c - 1))
                if quad == 2:
                    wait(pe, xn_t_ready[1], at.count(c - 1))
                for t in range(TT):
                    for lane in range(LANES):
                        k = LANES * quad + lane
                        mm = pe.matmul(pv_bank[g][VCOLS * lane:VCOLS * (lane + 1), 0:S],
                                       v_ops[at.stage(c)][:, t, k, :], probs[:, k % RING, t],
                                       start=first and t == 0, stop=not first and t == TT - 1)
                mm.then_inc(pv_done[quad], 1)

            def turn_pv(at):
                wait(pe, pv_copied[1], at.count(-1))
                for t in range(TT):
                    for g in range(2):
                        n = 2 * t + g
                        mm = pe.transpose(post_bank[:, n * P:(n + 1) * P], pv_t[:, g, t * P:(t + 1) * P], ident[:, :])
                mm.then_inc(pv_turned, 1)

            def turn_attn(at):
                wait(pe, attn_done, at.count(-1))
                for t in range(TT):
                    mm = pe.transpose(post_bank[:, t * P:(t + 1) * P],
                                      attn[:, 2 * t:2 * t + 2].rearrange("p g s l d -> p (g s l d)"), ident[:, :])
                mm.then_inc(attn_turned, 1)

            def project_attn(at):
                wait(pe, attn_t_ready, at.count(-1))
                for t in range(TT):
                    mm = pe.matmul(post_bank[:, t * P:(t + 1) * P], attn_t[:, t * P:(t + 1) * P], wo[:, :],
                                   start=True, stop=True)
                mm.then_inc(attn_proj, 1)

            def turn_xn2(at):
                wait(pe, xn_done[1], at.count(-1))
                for t in range(TT):
                    mm = pe.transpose(post_bank[:, t * P:(t + 1) * P], xn[:, 1, t], ident[:, :])
                mm.then_inc(xn_turned[1], 1)

            def project_gate_up(at, n):
                wait(pe, xn_t_ready[1], at.count(-1))
                to = chunk_bank[n]
                for i in range(2):
                    mm = pe.matmul(to[:, i * S:(i + 1) * S], wgu[:, n, i], xn_t[:, 1], start=True, stop=True)
                mm.then_inc(gate_up[n], 1)

            def project_down(at, t):
                for n in range(CH):
                    if t == 0:
                        wait(pe, hidden_done[n], at.count(-1))
                    mm = pe.matmul(chunk_bank[0][:, t * P:(t + 1) * P], hidden[:, n, t * P:(t + 1) * P], wd[:, n],
                                   start=n == 0, stop=n == CH - 1)
                if t == TT - 1:
                    mm.then_inc(down_proj, 1)

            start = Step(0, 0)
            pe.wait_ge(wk_in, 16)
            project_k(start, 0)
            pe.wait_ge(ident_ready, 2)
            turn_xn(start, 0)
            project_k(start, 1)
            pe.wait_ge(wq_in, 16)
            project_q(start, 0)
            pe.wait_ge(wv_in, 16)
            project_v(start, 0)
            turn_xn(start, 1)
            project_q(start, 1)
            for k in range(HEADS):
                max_scores(start, 0, k)
                if k == 1:
                    project_v(start, 1)
                if k == HALF + 1:
                    pe.wait_ge(v_ready, 2)
                    turn_max(start, 0, 0)
            pe.wait_ge(k_filled, 1)

            def step(at, before):
                for k in range(0, 2):
                    scores(at, k)
                    max_scores(at, 1, k)
                if before:
                    times_v(at, -1, 3)
                scores(at, 2)
                max_scores(at, 1, 2)
                project_k(at, 2)
                scores(at, 3)
                max_scores(at, 1, 3)
                turn_max(at, 0, 1)
                scores(at, 4)
                max_scores(at, 1, 4)
                if before:
                    turn_pv(at)
                scores(at, 5)
                max_scores(at, 1, 5)
                times_v(at, 0, 0)
                scores(at, 6)
                max_scores(at, 1, 6)
                if before:
                    turn_attn(at)
                scores(at, 7)
                max_scores(at, 1, 7)
                turn_xn(at, 2)
                if before:
                    project_attn(at)
                max_scores(at, 1, 8)
                scores(at, 8)
                project_q(at, 2)
                times_v(at, 0, 1)
                max_scores(at, 1, 9)
                scores(at, 9)
                project_v(at, 2)
                turn_max(at, 1, 0)
                scores(at, 10)
                max_scores(at, 1, 10)
                scores(at, 11)
                if before:
                    turn_xn2(at)
                max_scores(at, 1, 11)
                scores(at, 12)
                max_scores(at, 1, 12)
                if before:
                    wait(pe, max_t_ready[0], at.count(1))
                    project_gate_up(at, 1)
                scores(at, 13)
                if before:
                    wait(pe, v_ready, at.count(2))
                    project_gate_up(at, 2)
                max_scores(at, 1, 13)
                if before:
                    wait(pe, pv_copied[0], at.count(0))
                    project_gate_up(at, 0)
                scores(at, 14)
                times_v(at, 0, 2)
                for k in range(14, 16):
                    max_scores(at, 1, k)
                scores(at, 15)
                if before:
                    project_down(at, 0)
                    project_down(at, 1)
                else:
                    pe.wait_ge(k_filled, STAGES)
                    pe.wait_ge(wo_in, 16)
                    pe.wait_ge(weights_ready, 2)

            def last_heads(at):
                scores(at, 0)
                times_v(at, -1, 3)
                scores(at, 1)
                turn_max(at, 0, 1)
                scores(at, 2)
                turn_pv(at)
                for k in range(3, 7):
                    scores(at, k)
                turn_attn(at)
                scores(at, 7)
                times_v(at, 0, 0)
                project_attn(at)
                for k in range(8, 10):
                    scores(at, k)
                times_v(at, 0, 1)
                for k in range(10, 13):
                    scores(at, k)
                turn_xn2(at)
                for k in range(13, 16):
                    scores(at, k)
                times_v(at, 0, 2)

            def finish(at, previous):
                times_v(at, -1, 3)
                wait(pe, pv_copied[0], B)
                project_gate_up(previous, 0)
                turn_pv(at)
                project_gate_up(previous, 1)
                turn_attn(at)
                project_gate_up(previous, 2)
                project_attn(at)
                project_down(previous, 0)
                project_down(previous, 1)
                turn_xn2(at)
                project_gate_up(at, 1)
                project_gate_up(at, 2)
                wait(pe, y_done, B - 1)
                project_gate_up(at, 0)
                project_down(at, 0)
                project_down(at, 1)

            steps(pe, step, last_heads, finish, 1, 16, K_SPREAD, Q_SPREAD)

        @block.scalar
        def _(act):
            def part1_k(at, c):
                wait(act, k_proj, at.count(c))
                wait(act, k_spread, at.count(c - STAGES, K_SPREAD))
                act.activation(k_parts[:, at.stage(c), 0], proj_bank[c][:, 0:S], ACT.Copy).then_inc(k_part1, 1)

            def part2_k(at, c):
                wait(act, k_rest_done, at.count(c))
                act.activation(k_parts[:, at.stage(c), 1], k_rest[:, :], ACT.Copy).then_inc(k_part2, 1)

            def copy_xn_t(at, c, norm):
                wait(act, xn_turned[norm], at.count(c))
                act.activation(xn_t[:, norm], (post_bank if norm else proj_bank[c])[:, 0:S], ACT.Copy)\
                    .then_inc(xn_t_ready[norm], 1)

            def part1_q(at, c):
                wait(act, q_proj, at.count(c))
                wait(act, q_spread, at.count(c - STAGES, Q_SPREAD))
                act.activation(q_parts[:, at.stage(c), 0], proj_bank[c][:, 0:S], ACT.Copy).then_inc(q_part1, 1)

            def part2_q(at, c):
                wait(act, q_rest_done, at.count(c))
                act.activation(q_parts[:, at.stage(c), 1], q_rest[:, :], ACT.Copy).then_inc(q_part2, 1)

            def place_v(at, c):
                wait(act, v_proj, at.count(c))
                wait(act, pv_done[3], at.count(c - STAGES))
                to = v_ops[at.stage(c)][:, :, :, :].rearrange("p t (g s l) c -> p (t g) s l c", g=2, s=2)
                of = proj_bank[c][:, 0:TT * D].rearrange("p (n s l d) -> p n s l d", s=2, l=LANES, d=DK)
                for s in range(2):
                    ins = act.activation(to[:, :, s, :, DK * s:DK * (s + 1)], of[:, :, s], ACT.Copy)
                ins.then_inc(v_ready, 1)

            def copy_max_t(at, c, g):
                wait(act, max_turned[g], at.count(c))
                act.activation(max_t[g][:, :], bank_a[:, :].bitcast(BF16)[0:2 * HALF, 0:S], ACT.Copy)\
                    .then_inc(max_t_ready[g], 1)

            def exp(at, k):
                if k % LANES == 0:
                    quad = k // LANES
                    if quad >= 2:
                        wait(act, pv_done[quad - 2], at.count(0))
                    else:
                        wait(act, pv_done[quad + 2], at.count(-1))
                wait(act, scores_ready[k], at.count(0))
                act.activation(probs[:, k % RING].rearrange("p t s -> p (t s)"), score_bank[k % 2][:, :], ACT.Exp,
                               scale=SCALE).then_inc(probs_ready[k], 1)

            def copy_pv(at, c, g):
                wait(act, pv_done[2 * g + 1], at.count(c))
                act.activation(pv_t[:, g], pv_bank[g][:, 0:S], ACT.Copy).then_inc(pv_copied[g], 1)

            def copy_attn_t(at):
                wait(act, attn_turned, at.count(-1))
                act.activation(attn_t[:, :], post_bank[:, 0:S], ACT.Copy).then_inc(attn_t_ready, 1)

            def gate_tanh(at, n):
                wait(act, gate_up[n], at.count(-1))
                act.activation(tanh[:, n], chunk_bank[n][:, 0:S], ACT.Tanh, scale=0.5 * WEIGHT_SCALE)\
                    .then_inc(tanh_ready[n], 1)

            def take_gate_up():
                act.wait_ge(wgu_in, 16)
                act.activation(wgu[:, :, :, :], wgu_int[:, :, :, :], ACT.Copy).then_inc(weights_ready, 1)

            def take_down():
                act.wait_ge(wd_in, 16)
                act.activation(wd[:, :, :], wd_int[:, :, :], ACT.Copy).then_inc(weights_ready, 1)

            def fill_shift(i):
                act.activation(k_ops[i][SHIFT_ROW:ROWS].rearrange("p h s -> p (h s)").bitcast(F32),
                               ident[SHIFT_ROW:ROWS, 0:1].broadcast_to([2, HEADS * S // 2]), ACT.Copy,
                               bias=ONES_PAIR, scale=0.0).then_inc(k_filled, 1)

            act.dma_start(wk[:, :], wkT).then_inc(wk_in, 16)
            act.dma_start(wq[:, :], wqT).then_inc(wq_in, 16)
            start = Step(0, 0)
            act.wait_ge(ident_ready, 1)
            act.activation(tanh[:, 0, 0:1], ident[:, 0:1], ACT.Exp).then_inc(table_loaded, 1)
            part1_k(start, 0)
            part2_k(start, 0)
            copy_xn_t(start, 0, 0)
            part1_k(start, 1)
            part1_q(start, 0)
            part2_q(start, 0)
            part2_k(start, 1)
            act.wait_ge(v_filled, 2)
            place_v(start, 0)
            copy_xn_t(start, 1, 0)
            part1_q(start, 1)
            part2_q(start, 1)
            act.wait_ge(v_filled, 4)
            place_v(start, 1)
            fill_shift(0)
            fill_shift(1)
            fill_shift(2)
            copy_max_t(start, 0, 0)
            act.wait_ge(v_filled, 2 * STAGES)

            def step(at, before):
                for k in range(0, 2):
                    exp(at, k)
                if not before:
                    take_down()
                exp(at, 2)
                if before:
                    copy_pv(at, -1, 1)
                part1_k(at, 2)
                for k in range(3, 5):
                    exp(at, k)
                copy_max_t(at, 0, 1)
                exp(at, 5)
                part2_k(at, 2)
                if before:
                    copy_attn_t(at)
                exp(at, 6)
                copy_xn_t(at, 2, 0)
                exp(at, 7)
                if not before:
                    take_gate_up()
                part1_q(at, 2)
                exp(at, 8)
                part2_q(at, 2)
                exp(at, 9)
                copy_max_t(at, 1, 0)
                exp(at, 10)
                if before:
                    copy_xn_t(at, -1, 1)
                place_v(at, 2)
                exp(at, 11)
                copy_pv(at, 0, 0)
                exp(at, 12)
                if before:
                    gate_tanh(at, 1)
                    gate_tanh(at, 2)
                exp(at, 13)
                if before:
                    gate_tanh(at, 0)
                for k in range(14, 16):
                    exp(at, k)

            def last_heads(at):
                exp(at, 0)
                copy_pv(at, -1, 1)
                for k in range(1, 5):
                    exp(at, k)
                copy_max_t(at, 0, 1)
                for k in range(5, 7):
                    exp(at, k)
                copy_attn_t(at)
                for k in range(7, 13):
                    exp(at, k)
                copy_xn_t(at, -1, 1)
                exp(at, 13)
                copy_pv(at, 0, 0)
                for k in range(14, 16):
                    exp(at, k)

            def finish(at, previous):
                copy_pv(at, -1, 1)
                gate_tanh(previous, 0)
                gate_tanh(previous, 1)
                copy_attn_t(at)
                gate_tanh(previous, 2)
                copy_xn_t(at, -1, 1)
                gate_tanh(at, 1)
                gate_tanh(at, 2)
                gate_tanh(at, 0)

            steps(act, step, last_heads, finish, 1, K_SPREAD, Q_SPREAD)

        @block.vector
        def _(dve):
            def norm_stats(at, c, norm):
                if norm == 0:
                    wait(dve, x_loaded, at.count(c, 16))
                else:
                    wait(dve, x1_done, at.count(c))
                for t in range(TT):
                    of = (x_in if norm == 0 else x1)[:, at.stage(c), t]
                    ins = dve.bn_stats(stats[:, norm, t], of)
                ins.then_inc(stats_done[norm], 1)

            def norm_moments(at, c, norm):
                settle(dve)
                wait(dve, stats_done[norm], at.count(c))
                if norm == 0:
                    wait(dve, xn_done[0], at.count(c - 1))
                for t in range(TT):
                    ins = dve.bn_aggr(moments[:, norm, t], stats[:, norm, t])
                ins.then_inc(moments_done[norm], 1)

            def add_eps(at, c, norm):
                settle(dve)
                wait(dve, moments_done[norm], at.count(c))
                dve.tensor_scalar(var_eps[:, norm], moments[:, norm, :, 1], EPS, None, ALU.add)\
                    .then_inc(var_done[norm], 1)

            def normalise_rows(at, c, norm):
                settle(dve)
                wait(dve, rstd_done[norm], at.count(c))
                if norm == 0:
                    wait(dve, xn_turned[0], at.count(c - 1))
                for t in range(TT):
                    of = (x_in if norm == 0 else x1)[:, at.stage(c), t]
                    ins = dve.tensor_scalar(xn[:, norm, t], of, moments[:, norm, t, 0:1], rstd[:, norm, t:t + 1],
                                            ALU.subtract, ALU.mult)
                ins.then_inc(xn_done[norm], 1)

            def rest_k(at, c):
                wait(dve, k_part1, at.count(c))
                dve.tensor_tensor(k_rest[:, :], proj_bank[c][:, 0:S], k_parts[:, at.stage(c), 0], ALU.subtract)\
                    .then_inc(k_rest_done, 1)

            def rest_q(at, c):
                wait(dve, q_part1, at.count(c))
                dve.tensor_tensor(q_rest[:, :], proj_bank[c][:, 0:S], q_parts[:, at.stage(c), 0], ALU.subtract)\
                    .then_inc(q_rest_done, 1)

            def head_max(at, c, k):
                wait(dve, max_scores_ready[k], at.count(c))
                dve.tensor_reduce(neg_max[:, k // HALF, :, k % HALF],
                                  max_bank[k % 2][:, :].rearrange("p (t s) -> p t s", t=TT), AX.X, ALU.max,
                                  negate=True).then_inc(max_done[k], 1)

            def part1_max(at, c, g):
                wait(dve, max_done[HALF * g + HALF - 1], at.count(c))
                dve.tensor_copy(max_parts[:, g, :, 0], neg_max[:, g]).then_inc(max_part1[g], 1)

            def part2_max(at, c, g):
                wait(dve, max_part1[g], at.count(c))
                dve.tensor_tensor(max_parts[:, g, :, 1], neg_max[:, g], max_parts[:, g, :, 0], ALU.subtract)\
                    .then_inc(max_part2[g], 1)

            turned = post_bank[:, :].rearrange("p (n l c) -> p n l c", l=LANES, c=VCOLS)

            def reciprocals(at):
                wait(dve, pv_turned, at.count(-1))
                dve.reciprocal(recip[:, :, :, :], turned[:, :, :, 2 * DK:2 * DK + 2]).then_inc(recip_done, 1)

            def normalise(at):
                wait(dve, recip_done, at.count(-1))
                for s in range(2):
                    ins = dve.tensor_tensor(attn[:, :, s], turned[:, :, :, DK * s:DK * (s + 1)],
                                            recip[:, :, :, s:s + 1].broadcast_to([P, 2 * TT, LANES, DK]), ALU.mult)
                ins.then_inc(attn_done, 1)

            def residual(at):
                wait(dve, attn_proj, at.count(-1))
                wait(dve, res_loaded, at.count(-1, 16))
                dve.tensor_tensor(x1[:, at.stage(-1)], post_bank[:, 0:TT * D].rearrange("p (t d) -> p t d", t=TT),
                                  x_res[:, at.stage(-1)], ALU.add).then_inc(x1_done, 1)

            def gate(at, n):
                both = chunk_bank[n]
                wait(dve, tanh_ready[n], at.count(-1))
                dve.scalar_tensor_tensor(out=gated[:, n], in0=tanh[:, n], scalar=1.0, in1=both[:, 0:S],
                                         op0=ALU.add, op1=ALU.mult).then_inc(gated_done[n], 1)

            def times_up(at, n):
                both = chunk_bank[n]
                wait(dve, gated_done[n], at.count(-1))
                dve.tensor_tensor(hidden[:, n], both[:, S:2 * S], gated[:, n], ALU.mult)\
                    .then_inc(hidden_done[n], 1)

            def output(at):
                wait(dve, down_proj, at.count(-1))
                dve.scalar_tensor_tensor(out=y[:, at.stage(-1)],
                                         in0=chunk_bank[0][:, 0:TT * D].rearrange("p (t d) -> p t d", t=TT),
                                         scalar=0.5 * WEIGHT_SCALE**3, in1=x1[:, at.stage(-1)],
                                         op0=ALU.mult, op1=ALU.add).then_inc(y_done, 1)

            def fill_k(i):
                dve.memset(k_ops[i][0:MAX_ROWS].rearrange("p h s -> p (h s)").bitcast(F32), 0.0)\
                    .then_inc(ops_filled[i], 1)

            def last_part(rest, parts, ready, done, n):
                dve.wait_ge(ready, n + 1)
                dve.tensor_tensor(parts[:, n, 2], rest[:, :], parts[:, n, 1], ALU.subtract).then_inc(done, 1)

            start = Step(0, 0)
            fill_k(0)
            norm_stats(start, 0, 0)
            norm_moments(start, 0, 0)
            add_eps(start, 0, 0)
            rest_k(start, 0)
            last_part(k_rest, k_parts, k_part2, k_part3, 0)
            normalise_rows(start, 0, 0)
            dve.wait_ge(mask_in, 16)
            dve.tensor_scalar(mask_f[:, :], mask_u8[:, :], -1.0, 3e38, ALU.add, ALU.mult).then_inc(mask_sub, 1)
            norm_stats(start, 1, 0)
            dve.wait_ge(mask_sub, 1)
            dve.tensor_scalar(mask_bias[:, :], mask_f[:, :], 1e3, None, ALU.mult).then_inc(mask_ready, 1)
            norm_moments(start, 1, 0)
            add_eps(start, 1, 0)
            rest_k(start, 1)
            rest_q(start, 0)
            last_part(q_rest, q_parts, q_part2, q_part3, 0)
            last_part(k_rest, k_parts, k_part2, k_part3, 1)
            normalise_rows(start, 1, 0)
            rest_q(start, 1)
            last_part(q_rest, q_parts, q_part2, q_part3, 1)
            for k in range(HEADS):
                head_max(start, 0, k)
                if k == HALF - 1:
                    part1_max(start, 0, 0)
                if k == HALF:
                    part2_max(start, 0, 0)

            def step(at, before):
                norm_stats(at, 2, 0)
                head_max(at, 1, 0)
                part1_max(at, 0, 1)
                norm_moments(at, 2, 0)
                head_max(at, 1, 1)
                part2_max(at, 0, 1)
                head_max(at, 1, 2)
                add_eps(at, 2, 0)
                head_max(at, 1, 3)
                rest_k(at, 2)
                head_max(at, 1, 4)
                if before:
                    reciprocals(at)
                    normalise(at)
                for k in range(5, 8):
                    head_max(at, 1, k)
                if before:
                    residual(at)
                    norm_stats(at, -1, 1)
                part1_max(at, 1, 0)
                if before:
                    norm_moments(at, -1, 1)
                head_max(at, 1, 8)
                if before:
                    add_eps(at, -1, 1)
                rest_q(at, 2)
                part2_max(at, 1, 0)
                head_max(at, 1, 9)
                if before:
                    normalise_rows(at, -1, 1)
                for k in range(10, 13):
                    head_max(at, 1, k)
                if before:
                    gate(at, 1)
                head_max(at, 1, 13)
                if before:
                    times_up(at, 1)
                    gate(at, 2)
                    gate(at, 0)
                    times_up(at, 0)
                    times_up(at, 2)
                for k in range(14, 16):
                    head_max(at, 1, k)
                if before:
                    output(at)

            def last_heads(at):
                part1_max(at, 0, 1)
                part2_max(at, 0, 1)
                reciprocals(at)
                normalise(at)
                residual(at)
                norm_stats(at, -1, 1)
                norm_moments(at, -1, 1)
                add_eps(at, -1, 1)
                normalise_rows(at, -1, 1)

            def finish(at, previous):
                reciprocals(at)
                normalise(at)
                gate(previous, 0)
                times_up(previous, 0)
                gate(previous, 1)
                times_up(previous, 1)
                residual(at)
                norm_stats(at, -1, 1)
                gate(previous, 2)
                norm_moments(at, -1, 1)
                add_eps(at, -1, 1)
                times_up(previous, 2)
                normalise_rows(at, -1, 1)
                output(previous)
                gate(at, 1)
                times_up(at, 1)
                gate(at, 2)
                times_up(at, 2)
                gate(at, 0)
                times_up(at, 0)
                output(at)

            steps(dve, step, last_heads, finish, 1, 16)

        @block.gpsimd
        def _(pool):
            def inverse_root(at, c, norm):
                wait(pool, var_done[norm], at.count(c))
                pool.tensor_tensor(rstd[:, norm], var_eps[:, norm], minus_half[:, :], ALU.pow)\
                    .then_inc(rstd_done[norm], 1)

            def normalise(at, c):
                settle(pool)
                wait(pool, rstd_done[0], at.count(c))
                wait(pool, xn_turned[0], at.count(c - 1))
                for t in range(TT):
                    ins = pool.tensor_scalar(xn[:, 0, t], x_in[:, at.stage(c), t], moments[:, 0, t, 0:1],
                                             rstd[:, 0, t:t + 1], ALU.subtract, ALU.mult)
                ins.then_inc(xn_done[0], 1)

            def last_part_k(at, c):
                wait(pool, k_part2, at.count(c))
                pool.tensor_tensor(k_parts[:, at.stage(c), 2], k_rest[:, :], k_parts[:, at.stage(c), 1], ALU.subtract)\
                    .then_inc(k_part3, 1)

            def last_part_q(at, c):
                wait(pool, q_part2, at.count(c))
                pool.tensor_tensor(q_parts[:, at.stage(c), 2], q_rest[:, :], q_parts[:, at.stage(c), 1], ALU.subtract)\
                    .then_inc(q_part3, 1)

            def fill_q(i):
                pool.memset(q_ops[i][0:MAX_ROWS].rearrange("p h s -> p (h s)").bitcast(F32), ONES_PAIR)\
                    .then_inc(ops_filled[i], 1)

            pool.memset(minus_half[:, :], -0.5).then_inc(consts_ready, 1)
            pool.memset(ident[:, :], 0.0).then_inc(ident_zero, 1)
            pool.memset(ident_bf[:, :], 0.0).then_inc(ident_zero, 1)
            pool.wait_ge(ident_zero, 2)
            for m in (ident, ident_bf):
                pool.affine_select(out=m[:, :], in_=m[:, :], compare_op=ALU.not_equal, fill=1.0, base=0,
                                   pattern=[[-1, P]], channel_multiplier=1).then_inc(ident_ready, 1)
            def fill_k(i):
                pool.memset(k_ops[i][0:MAX_ROWS].rearrange("p h s -> p (h s)").bitcast(F32), 0.0)\
                    .then_inc(ops_filled[i], 1)

            def fill_v(i):
                pool.memset(v_ops[i][:, :, :, :], 0.0).then_inc(v_zero, 1)
                pool.wait_ge(v_zero, i + 1)
                for s in range(2):
                    to = v_ops[i][:, :, :, :].rearrange("p t (g s l) c -> p (t g) s l c", g=2, s=2)
                    pool.memset(to[:, :, s, :, 2 * DK + s:2 * DK + s + 1], 1.0).then_inc(v_filled, 1)

            start = Step(0, 0)
            fill_q(0)
            pool.wait_ge(consts_ready, 1)
            inverse_root(start, 0, 0)
            fill_v(0)
            inverse_root(start, 1, 0)
            fill_k(1)
            fill_q(1)
            fill_v(1)
            fill_k(2)
            fill_q(2)
            fill_v(2)

            def step(at, before):
                inverse_root(at, 2, 0)
                normalise(at, 2)
                last_part_k(at, 2)
                if before:
                    inverse_root(at, -1, 1)
                last_part_q(at, 2)

            def last_heads(at):
                inverse_root(at, -1, 1)

            def finish(at, previous):
                inverse_root(at, -1, 1)

            steps(pool, step, last_heads, finish, 1)


INPUTS = ("x", "ctxT", "mask", "wqT", "wkT", "wvT", "woT", "wguT", "wdT")


def kernel(x, ctx_1024, mask_BxS2_bf1, L0_xattn_w_q, L0_xattn_w_k, L0_xattn_w_v, L0_xattn_w_o, L0_ffn_w_gate,
           L0_ffn_w_up, L0_ffn_w_down):
    import concourse.bacc as bacc
    import numpy as np
    from concourse.bass_utils import run_bass_kernel_spmd

    def by_place(w):
        w = np.asarray(w)
        return w.reshape(HEADS, DK, w.shape[1]).transpose(2, 1, 0).reshape(w.shape[1], HEADS * DK)

    ctx = np.asarray(ctx_1024)
    gate, up, down = (np.asarray(w) for w in (L0_ffn_w_gate, L0_ffn_w_up, L0_ffn_w_down))
    chunks = gate.shape[0] // P
    arrays = {
        "x": np.asarray(x),
        "ctxT": ctx.transpose(0, 2, 1),
        "mask": np.asarray(mask_BxS2_bf1).view(np.uint8),
        "wqT": by_place(L0_xattn_w_q),
        "wkT": by_place(L0_xattn_w_k),
        "wvT": np.asarray(L0_xattn_w_v).T,
        "woT": np.asarray(L0_xattn_w_o).T,
        "wguT": np.stack([gate, up]).reshape(2, chunks, P, -1).transpose(3, 1, 0, 2),
        "wdT": down.reshape(-1, chunks, P).transpose(2, 1, 0),
    }
    arrays = {name: np.ascontiguousarray(a) for name, a in arrays.items()}
    nc = bacc.Bacc("TRN2", target_bir_lowering=False, num_devices=1)
    aps = [nc.dram_tensor(name, arrays[name].shape, mybir.dt.from_np(arrays[name].dtype), kind="ExternalInput").ap()
           for name in INPUTS]
    out = nc.dram_tensor("out", arrays["x"].shape, F32, kind="ExternalOutput").ap()
    build(nc, *aps, out)
    r = run_bass_kernel_spmd(nc, [arrays], core_ids=[0])
    return r.results[0]["out"]
```
